# Optimizing a Trainium2 kernel written in Bass

```python
import numpy as np
import jax
import jax.numpy as jnp

def _softmax(x, axis=-1):
    return jax.nn.softmax(x, axis=axis)

def _gelu(x):
    return jax.nn.gelu(x, approximate=True)

def _silu(x):
    return jax.nn.silu(x)

def _sigmoid(x):
    return jax.nn.sigmoid(x)

def _layernorm(x, axis=-1, eps=1e-05):
    m = jnp.mean(x, axis=axis, keepdims=True)
    v = jnp.var(x, axis=axis, keepdims=True)
    return (x - m) / jnp.sqrt(v + eps)

def _scatter_add(tgt, idx, src, axis=0):
    return tgt.at[idx].add(src)

def _segment_sum(src, seg, n):
    return jax.ops.segment_sum(src, seg, n)
kernel_name = 'mk_gnn_ffn_d2_gnn_r32_c77c41'

def setup_inputs(seed: int=0):
    np.random.seed(seed)
    _w = jnp.asarray

    def _rec_inputs():
        import jax
        import jax.numpy as jnp
        _gk = jax.random.key(seed)
        x = -0.0003713 + 1 * jax.random.normal(jax.random.fold_in(_gk, 1), (3125, 256), jnp.float32)
        src = jax.random.randint(jax.random.fold_in(_gk, 2), (50000,), 0, 3125, jnp.int32)
        dst = jnp.minimum((3125 * jax.random.uniform(jax.random.fold_in(_gk, 3), (50000,)) ** 2.0).astype(jnp.int32), 99999)
        _o = jnp.argsort(dst, stable=True)
        src = src[_o]
        dst = dst[_o]
        edge_type_400 = jax.random.randint(jax.random.fold_in(_gk, 12), (50000,), 0, 400, jnp.int32)
        return (x, src, dst, edge_type_400)
    x, src, dst, edge_type_400 = _rec_inputs()

    def _L0_gnn_setup():
        import jax, jax.numpy as jnp
        import numpy as np
        N = 50000
        D = 256
        E = 10000
        R = 400

        def _mgcn_conv(x, edge_index, edge_type, rel, W_in, W_out, W_loop, b, n):
            src, dst = (edge_index[0], edge_index[1])
            e = edge_index.shape[1]
            half = e // 2
            m = x[src] * rel[edge_type]
            m = jnp.concatenate([m[:half] @ W_in, m[half:] @ W_out], 0)
            deg = jax.ops.segment_sum(jnp.ones((e,), x.dtype), dst, num_segments=n)
            norm = 1.0 / jnp.maximum(deg, 1.0)
            agg = jax.ops.segment_sum(m * norm[dst][:, None], dst, num_segments=n)
            return jnp.tanh(agg + x @ W_loop + b)
        key = jax.random.key(seed)
        ks = jax.random.split(key, 12)
        s = 0.05
        w = lambda k, shp: jax.random.normal(k, shp, jnp.float32) * s
        return {'emb': jax.random.normal(ks[0], (N, D), jnp.float32), 'edge_index': jax.random.randint(ks[1], (2, E), 0, N), 'edge_type': jax.random.randint(ks[2], (E,), 0, R), 'rel1': w(ks[3], (R, D)), 'W_in1': w(ks[4], (D, D)), 'W_out1': w(ks[5], (D, D)), 'W_loop1': w(ks[6], (D, D)), 'b1': jnp.zeros((D,), jnp.float32), 'rel2': w(ks[7], (R, D)), 'W_in2': w(ks[8], (D, D)), 'W_out2': w(ks[9], (D, D)), 'W_loop2': w(ks[10], (D, D)), 'b2': jnp.zeros((D,), jnp.float32), 'res': jnp.array([0.1], jnp.float32), 'mu_w': w(ks[11], (D, D)), 'mu_b': jnp.zeros((D,), jnp.float32), 'num_nodes': N}
    _L0_gnn_all = _L0_gnn_setup()
    _L0_gnn_in = {k: v for k, v in _L0_gnn_all.items() if k in ('rel1', 'W_in1', 'W_out1', 'W_loop1', 'b1', 'rel2', 'W_in2', 'W_out2', 'W_loop2', 'b2', 'res', 'mu_w', 'mu_b')}
    del _L0_gnn_all

    def _L0_ffn_setup():
        import jax, jax.numpy as jnp
        import numpy as np
        B, S, H, F, E, K = (8, 128, 256, 512, 16, 2)
        EPS = 1e-05
        key = jax.random.key(seed)
        ks = jax.random.split(key, 9)
        sc = 0.02
        return {'x': jax.random.normal(ks[0], (B, S, H), dtype=jnp.float32), 'gate_w': jax.random.normal(ks[1], (H, E), dtype=jnp.float32) * sc, 'gate_b': jnp.zeros((E,), dtype=jnp.float32), 'w1': jax.random.normal(ks[2], (E, H, F), dtype=jnp.float32) * sc, 'b1': jnp.zeros((E, F), dtype=jnp.float32), 'w2': jax.random.normal(ks[3], (E, F, H), dtype=jnp.float32) * sc, 'b2': jnp.zeros((E, H), dtype=jnp.float32), 'gamma': jnp.ones((H,), dtype=jnp.float32), 'beta': jnp.zeros((H,), dtype=jnp.float32)}
    _L0_ffn_all = _L0_ffn_setup()
    _L0_ffn_in = {k: v for k, v in _L0_ffn_all.items() if k in ('gate_w', 'gate_b', 'w1', 'b1', 'w2', 'b2', 'gamma', 'beta')}
    del _L0_ffn_all

    def _L1_gnn_setup():
        import jax, jax.numpy as jnp
        import numpy as np
        N = 10000
        E = 9375
        D = 256
        key = jax.random.key(seed)
        k1, k2, k3, k4 = jax.random.split(key, 4)
        x = jax.random.normal(k1, (N, D), dtype=jnp.float32)
        edge_index = jax.random.randint(k2, (2, E), 0, N, dtype=jnp.int32)
        s = 1.0 / np.sqrt(D)
        W1 = jax.random.uniform(k3, (D, D), jnp.float32, -s, s)
        b1 = jnp.zeros((D,), jnp.float32)
        W2 = jax.random.uniform(k4, (D, D), jnp.float32, -s, s)
        b2 = jnp.zeros((D,), jnp.float32)
        return {'x': x, 'W1': W1, 'b1': b1, 'W2': W2, 'b2': b2, 'edge_index': edge_index}
    _L1_gnn_all = _L1_gnn_setup()
    _L1_gnn_in = {k: v for k, v in _L1_gnn_all.items() if k in ('W1', 'b1', 'W2', 'b2')}
    del _L1_gnn_all

    def _L1_ffn_setup():
        import jax, jax.numpy as jnp
        import numpy as np
        DIM = 256
        H = 8
        D = 64
        G = 64
        INNER = H * D
        SCALE = D ** (-0.5)
        key = jax.random.key(seed)
        ks = jax.random.split(key, 12)
        B, N = (4, 512)
        x = jax.random.normal(ks[0], (B, N, DIM), dtype=jnp.float32)
        s = lambda fan_in: 1.0 / np.sqrt(fan_in)
        W_fx = jax.random.normal(ks[1], (DIM, INNER), dtype=jnp.float32) * s(DIM)
        b_fx = jnp.zeros((INNER,), dtype=jnp.float32)
        W_x = jax.random.normal(ks[2], (DIM, INNER), dtype=jnp.float32) * s(DIM)
        b_x = jnp.zeros((INNER,), dtype=jnp.float32)
        A = jax.random.normal(ks[3], (G, D), dtype=jnp.float32)
        Q, _ = jnp.linalg.qr(A.T)
        W_slice = Q[:, :G].astype(jnp.float32)
        b_slice = jnp.zeros((G,), dtype=jnp.float32)
        W_q = jax.random.normal(ks[4], (D, D), dtype=jnp.float32) * s(D)
        W_k = jax.random.normal(ks[5], (D, D), dtype=jnp.float32) * s(D)
        W_v = jax.random.normal(ks[6], (D, D), dtype=jnp.float32) * s(D)
        W_out = jax.random.normal(ks[7], (INNER, DIM), dtype=jnp.float32) * s(INNER)
        b_out = jnp.zeros((DIM,), dtype=jnp.float32)
        temperature = jnp.ones((1, H, 1, 1), dtype=jnp.float32) * 0.5
        return {'x': x, 'W_fx': W_fx, 'b_fx': b_fx, 'W_x': W_x, 'b_x': b_x, 'W_slice': W_slice, 'b_slice': b_slice, 'W_q': W_q, 'W_k': W_k, 'W_v': W_v, 'W_out': W_out, 'b_out': b_out, 'temperature': temperature}
    _L1_ffn_all = _L1_ffn_setup()
    _L1_ffn_in = {k: v for k, v in _L1_ffn_all.items() if k in ('W_fx', 'b_fx', 'W_x', 'b_x', 'W_slice', 'b_slice', 'W_q', 'W_k', 'W_v', 'W_out', 'b_out', 'temperature')}
    del _L1_ffn_all
    return {'x': x, 'src': src, 'dst': dst, 'edge_type_400': edge_type_400, 'L0_gnn_rel1': _L0_gnn_in['rel1'], 'L0_gnn_W_in1': _L0_gnn_in['W_in1'], 'L0_gnn_W_out1': _L0_gnn_in['W_out1'], 'L0_gnn_W_loop1': _L0_gnn_in['W_loop1'], 'L0_gnn_b1': _L0_gnn_in['b1'], 'L0_gnn_rel2': _L0_gnn_in['rel2'], 'L0_gnn_W_in2': _L0_gnn_in['W_in2'], 'L0_gnn_W_out2': _L0_gnn_in['W_out2'], 'L0_gnn_W_loop2': _L0_gnn_in['W_loop2'], 'L0_gnn_b2': _L0_gnn_in['b2'], 'L0_gnn_res': _L0_gnn_in['res'], 'L0_gnn_mu_w': _L0_gnn_in['mu_w'], 'L0_gnn_mu_b': _L0_gnn_in['mu_b'], 'L0_ffn_gate_w': _L0_ffn_in['gate_w'], 'L0_ffn_gate_b': _L0_ffn_in['gate_b'], 'L0_ffn_w1': _L0_ffn_in['w1'], 'L0_ffn_b1': _L0_ffn_in['b1'], 'L0_ffn_w2': _L0_ffn_in['w2'], 'L0_ffn_b2': _L0_ffn_in['b2'], 'L0_ffn_gamma': _L0_ffn_in['gamma'], 'L0_ffn_beta': _L0_ffn_in['beta'], 'L1_gnn_W1': _L1_gnn_in['W1'], 'L1_gnn_b1': _L1_gnn_in['b1'], 'L1_gnn_W2': _L1_gnn_in['W2'], 'L1_gnn_b2': _L1_gnn_in['b2'], 'L1_ffn_W_fx': _L1_ffn_in['W_fx'], 'L1_ffn_b_fx': _L1_ffn_in['b_fx'], 'L1_ffn_W_x': _L1_ffn_in['W_x'], 'L1_ffn_b_x': _L1_ffn_in['b_x'], 'L1_ffn_W_slice': _L1_ffn_in['W_slice'], 'L1_ffn_b_slice': _L1_ffn_in['b_slice'], 'L1_ffn_W_q': _L1_ffn_in['W_q'], 'L1_ffn_W_k': _L1_ffn_in['W_k'], 'L1_ffn_W_v': _L1_ffn_in['W_v'], 'L1_ffn_W_out': _L1_ffn_in['W_out'], 'L1_ffn_b_out': _L1_ffn_in['b_out'], 'L1_ffn_temperature': _L1_ffn_in['temperature']}

def reference(x, src, dst, edge_type_400, L0_gnn_rel1, L0_gnn_W_in1, L0_gnn_W_out1, L0_gnn_W_loop1, L0_gnn_b1, L0_gnn_rel2, L0_gnn_W_in2, L0_gnn_W_out2, L0_gnn_W_loop2, L0_gnn_b2, L0_gnn_res, L0_gnn_mu_w, L0_gnn_mu_b, L0_ffn_gate_w, L0_ffn_gate_b, L0_ffn_w1, L0_ffn_b1, L0_ffn_w2, L0_ffn_b2, L0_ffn_gamma, L0_ffn_beta, L1_gnn_W1, L1_gnn_b1, L1_gnn_W2, L1_gnn_b2, L1_ffn_W_fx, L1_ffn_b_fx, L1_ffn_W_x, L1_ffn_b_x, L1_ffn_W_slice, L1_ffn_b_slice, L1_ffn_W_q, L1_ffn_W_k, L1_ffn_W_v, L1_ffn_W_out, L1_ffn_b_out, L1_ffn_temperature):
    import jax
    import jax.numpy as jnp

    def _L0_gnn_ref(emb, edge_index, edge_type, rel1, W_in1, W_out1, W_loop1, b1, rel2, W_in2, W_out2, W_loop2, b2, res, mu_w, mu_b, num_nodes):
        import jax, jax.numpy as jnp
        import numpy as np
        N = 50000
        D = 256
        E = 10000
        R = 400

        def _mgcn_conv(x, edge_index, edge_type, rel, W_in, W_out, W_loop, b, n):
            src, dst = (edge_index[0], edge_index[1])
            e = edge_index.shape[1]
            half = e // 2
            m = x[src] * rel[edge_type]
            m = jnp.concatenate([m[:half] @ W_in, m[half:] @ W_out], 0)
            deg = jax.ops.segment_sum(jnp.ones((e,), x.dtype), dst, num_segments=n)
            norm = 1.0 / jnp.maximum(deg, 1.0)
            agg = jax.ops.segment_sum(m * norm[dst][:, None], dst, num_segments=n)
            return jnp.tanh(agg + x @ W_loop + b)
        h = emb + res * _mgcn_conv(emb, edge_index, edge_type, rel1, W_in1, W_out1, W_loop1, b1, num_nodes)
        h = h + res * _mgcn_conv(h, edge_index, edge_type, rel2, W_in2, W_out2, W_loop2, b2, num_nodes)
        return h @ mu_w + mu_b

    def _L0_ffn_ref(x, gate_w, gate_b, w1, b1, w2, b2, gamma, beta):
        import jax, jax.numpy as jnp
        import numpy as np
        B, S, H, F, E, K = (8, 128, 256, 512, 16, 2)
        EPS = 1e-05
        gate_logits = x @ gate_w + gate_b
        topk_vals, topk_idx = jax.lax.top_k(gate_logits, K)
        topk_w = jax.nn.softmax(topk_vals, axis=-1)
        h = jax.nn.relu(jnp.einsum('bsh,ehf->bsef', x, w1) + b1)
        expert_out = jnp.einsum('bsef,efh->bseh', h, w2) + b2
        sel = jnp.take_along_axis(expert_out, topk_idx[:, :, :, None], axis=2)
        moe = jnp.sum(topk_w[..., None] * sel, axis=2)
        y = x + moe
        mu = jnp.mean(y, axis=-1, keepdims=True)
        var = jnp.var(y, axis=-1, keepdims=True)
        return (y - mu) / jnp.sqrt(var + EPS) * gamma + beta

    def _L1_gnn_ref(x, W1, b1, W2, b2, edge_index):
        import jax, jax.numpy as jnp
        import numpy as np
        N = 10000
        E = 9375
        D = 256
        n = x.shape[0]
        loops = jnp.arange(n, dtype=edge_index.dtype)
        src = jnp.concatenate([edge_index[0], loops])
        dst = jnp.concatenate([edge_index[1], loops])
        deg = jax.ops.segment_sum(jnp.ones(src.shape[0], x.dtype), dst, num_segments=n)
        dinv = jnp.where(deg > 0, jax.lax.rsqrt(jnp.maximum(deg, 1e-12)), 0.0)
        norm = dinv[src] * dinv[dst]

        def gcn_conv(h, W, b):
            m = (h @ W)[src] * norm[:, None]
            return jax.ops.segment_sum(m, dst, num_segments=n) + b
        x1 = gcn_conv(x, W1, b1)
        x1 = x1 / jnp.maximum(jnp.linalg.norm(x1, axis=-1, keepdims=True), 1e-12)
        x2 = gcn_conv(x1, W2, b2)
        return x2 + x

    def _L1_ffn_ref(x, W_fx, b_fx, W_x, b_x, W_slice, b_slice, W_q, W_k, W_v, W_out, b_out, temperature):
        import jax, jax.numpy as jnp
        import numpy as np
        DIM = 256
        H = 8
        D = 64
        G = 64
        INNER = H * D
        SCALE = D ** (-0.5)
        B, N, _ = x.shape
        fx_mid = (x @ W_fx + b_fx).reshape(B, N, H, D).transpose(0, 2, 1, 3)
        x_mid = (x @ W_x + b_x).reshape(B, N, H, D).transpose(0, 2, 1, 3)
        temp = jnp.clip(temperature, 0.1, 5.0)
        slice_weights = jax.nn.softmax((x_mid @ W_slice + b_slice) / temp, axis=-1)
        slice_norm = slice_weights.sum(axis=2)
        slice_token = jnp.einsum('bhnc,bhng->bhgc', fx_mid, slice_weights)
        slice_token = slice_token / (slice_norm[..., None] + 1e-05)
        q = slice_token @ W_q
        k = slice_token @ W_k
        v = slice_token @ W_v
        attn = jax.nn.softmax(jnp.einsum('bhgc,bhkc->bhgk', q, k) * SCALE, axis=-1)
        out_slice = jnp.einsum('bhgk,bhkc->bhgc', attn, v)
        out_x = jnp.einsum('bhgc,bhng->bhnc', out_slice, slice_weights)
        out_x = out_x.transpose(0, 2, 1, 3).reshape(B, N, INNER)
        return out_x @ W_out + b_out
    edge_index = jnp.stack([src, dst])
    x = x + _L0_gnn_ref(_layernorm(x, axis=-1), edge_index, edge_type_400, L0_gnn_rel1, L0_gnn_W_in1, L0_gnn_W_out1, L0_gnn_W_loop1, L0_gnn_b1, L0_gnn_rel2, L0_gnn_W_in2, L0_gnn_W_out2, L0_gnn_W_loop2, L0_gnn_b2, L0_gnn_res, L0_gnn_mu_w, L0_gnn_mu_b, 3125)
    x = x + _L0_ffn_ref(_layernorm(x, axis=-1)[None], L0_ffn_gate_w, L0_ffn_gate_b, L0_ffn_w1, L0_ffn_b1, L0_ffn_w2, L0_ffn_b2, L0_ffn_gamma, L0_ffn_beta)[0]
    x = x + _L1_gnn_ref(_layernorm(x, axis=-1), L1_gnn_W1, L1_gnn_b1, L1_gnn_W2, L1_gnn_b2, edge_index)
    x = x + _L1_ffn_ref(_layernorm(x, axis=-1)[None], L1_ffn_W_fx, L1_ffn_b_fx, L1_ffn_W_x, L1_ffn_b_x, L1_ffn_W_slice, L1_ffn_b_slice, L1_ffn_W_q, L1_ffn_W_k, L1_ffn_W_v, L1_ffn_W_out, L1_ffn_b_out, L1_ffn_temperature)[0]
    return x

_drawn_inputs = setup_inputs


def setup_inputs(seed=0):
    import zlib

    import numpy as np

    out = dict(_drawn_inputs(seed))
    spreads = {'L0_gnn_b1': (0.0, 0.8),
     'L0_gnn_b2': (0.0, 0.8),
     'L0_gnn_mu_b': (0.0, 0.1),
     'L0_ffn_gate_b': (0.0, 0.1),
     'L0_ffn_b1': (0.0, 0.8),
     'L0_ffn_b2': (0.0, 0.1),
     'L0_ffn_gamma': (1.0, 0.2),
     'L0_ffn_beta': (0.0, 0.1),
     'L1_gnn_b1': (0.0, 0.8),
     'L1_gnn_b2': (0.0, 0.1),
     'L1_ffn_b_fx': (0.0, 0.1),
     'L1_ffn_b_x': (0.0, 0.8),
     'L1_ffn_b_slice': (0.0, 2.0),
     'L1_ffn_b_out': (0.0, 0.274),
     'L1_ffn_temperature': (0.5, 0.6)}
    factors = {'L0_gnn_rel1': 8.0,
     'L0_gnn_W_in1': 29.187,
     'L0_gnn_W_out1': 8.0,
     'L0_gnn_rel2': 8.0,
     'L0_gnn_W_in2': 29.039,
     'L0_gnn_W_out2': 8.0,
     'L1_gnn_W1': 8.0,
     'L1_gnn_W2': 7.245,
     'L1_ffn_W_x': 8.0,
     'L1_ffn_W_slice': 8.0,
     'L1_ffn_W_q': 8.0,
     'L1_ffn_W_k': 8.0}
    for name, (base, spread) in spreads.items():
        noise = np.random.default_rng([zlib.crc32(name.encode()), seed]).standard_normal(out[name].shape)
        drawn = base * np.exp(spread * noise) if base else spread * noise
        out[name] = jnp.asarray(drawn.astype(out[name].dtype))
    for name, factor in factors.items():
        out[name] = (out[name] * factor).astype(out[name].dtype)
    return out
```

```python
import concourse.bass as bass
from concourse import mybir
from contextlib import ExitStack, contextmanager
import numpy as np

P = 128
N, D = 3125, 256
KD = D // P
NT = -(-N // P)
NPAD = NT * P
CT = 5
CH = NT // CT
CN = CT * P
CB = CN // 2
LAST = N - (NT - 1) * P
EDGES = 50000
HALF = EDGES // 2
Q = 4
GE = Q * P
GH = -(-HALF // GE)
NG = 2 * GH
TAIL = HALF - (GH - 1) * GE
AW = NPAD + P
SLOTS = 2
RELS = 400
NE, F, TOPK = 16, 512, 2
KF = F // P
ST = (TOPK * N + NE * (P - 1)) // P
ST += ST % 2
SROWS = ST * P
SALL = SROWS + 2 * P
HEADS, HD, G = 8, 64, 64
INNER = HEADS * HD
PAIRS = HEADS // 2
LN_EPS, TOKEN_EPS = 1e-5, 1e-5
ATT_SCALE = HD ** -0.5

f32, i32, u32 = mybir.dt.float32, mybir.dt.int32, mybir.dt.uint32
ALU, ACT, AX = mybir.AluOpType, mybir.ActivationFunctionType, mybir.AxisListType.X
ds = bass.ds


class Chain:

    def __init__(self, eng, sem):
        self.eng, self.sem, self.base, self.k, self.off = eng, sem, 0, 0, None

    def __call__(self, ins):
        self.k += 1
        ins.then_inc(self.sem, 1)
        at = self.base + self.k
        self.eng.wait_ge(self.sem, at if self.off is None else self.off + at)

    @contextmanager
    def loop(self, n, per):
        self.base, self.k = self.base + self.k, 0
        with self.eng.Fori(0, n) as i:
            self.off = i * per if per else None
            yield i
        assert self.k == per, (self.k, per)
        self.base, self.k, self.off = self.base + n * per, 0, None


def gnn_ffn_kernel(nc, A, out):
    ctx = ExitStack()
    with ctx:
        ctx.enter_context(nc.allow_non_contiguous_dma(reason="biases turned on their way in"))
        def sb(name, shape, dt=f32):
            return ctx.enter_context(nc.sbuf_tensor(name, shape, dt))

        made = {}

        def sem(name):
            if name not in made:
                made[name] = ctx.enter_context(nc.semaphore(name))
            return made[name]

        def dram(name, shape):
            return nc.dram_tensor(name, shape, f32, kind="Internal").ap()

        X = sb("X", [P, NT, D])
        FT = sb("FT", [P, KD, NPAD])
        FTn = FT[:, :, :].rearrange("p k n -> p (k n)").rearrange("p (t d) -> p t d", d=D)
        ACC = sb("ACC", [P, KD * 2 * AW])
        acc = ACC[:, :].rearrange("p (k n) -> p k n", k=KD)
        acc4 = ACC[:, :].rearrange("p (k h n) -> p k h n", k=KD, h=2)
        acc_self = acc[:, :, 0:AW]
        NORM = sb("NORM", [P, AW])
        IOTA = sb("IOTA", [P, AW])
        idx_all = sb("idx_all", [P, NG, 2 * Q], i32)
        dst_all = sb("dst_all", [P, NG, Q])
        idx_slot = sb("idx_slot", [P, SLOTS, 2 * Q], i32)
        XG = sb("XG", [P, SLOTS, Q, D])
        RG = sb("RG", [P, SLOTS, Q, D])
        OH = sb("OH", [P, SLOTS, Q, P])
        OHX = sb("OHX", [P, Q, P])
        STG = sb("STG", [P, KD, CN])
        TNH = sb("TNH", [P, KD, CN])
        NODE = sb("NODE", [P, CT, D + 1])
        WB = sb("WB", [P, 3, KD, D])
        MUW = sb("MUW", [P, KD, D])
        MUB = sb("MUB", [P, D])
        BV = sb("BV", [P, KD])
        RES = sb("RES", [P, 1])
        ident = sb("ident", [P, P])
        ones = sb("ones", [P, P])
        zeros = sb("zeros", [P, D + 1])
        tri = sb("tri", [P, P])
        rowmask = sb("rowmask", [P, NT])
        trash = sb("trash", [P, NT, TOPK])
        stats = sb("stats", [P, NT, 6])
        mv = sb("mv", [P, NT, 2])
        rstd = sb("rstd", [P, NT])
        tmpn = sb("tmpn", [P, NT])
        DINV = sb("DINV", [P, NT])
        mv2 = sb("mv2", [P, NT, 2])
        shift = sb("shift", [P, NT])
        grp = sb("grp", [P, 4])
        gpart = sb("gpart", [P, 1])
        grow = sb("grow", [1, 4, NG])
        rows_i = sb("rows_i", [1, NG, 4], i32)
        bank = [ctx.enter_context(nc.psum_tensor(f"bank{b}", [P, 512], f32)) for b in range(8)]

        nat = ACC[0:NG, 0:4 * GE].bitcast(i32).rearrange("p (a e) -> p a e", a=4)
        natf = ACC[0:NG, 4 * GE:8 * GE].rearrange("p (a e) -> p a e", a=4)
        SWT = ACC[:, 0:PAIRS * NPAD].rearrange("p (a n) -> p a n", a=PAIRS)
        RR = ACC[:, 0:TOPK * NT * D].rearrange("p (a t d) -> p a t d", a=TOPK, t=NT)

        LOG = sb("LOG", [P, NT, NE])
        mx8 = sb("mx8", [P, NT, 8])
        mi8 = sb("mi8", [P, NT, 8], u32)
        topf = sb("topf", [P, NT, TOPK])
        topw = sb("topw", [P, NT, TOPK])
        i16 = sb("i16", [P, NE])
        pos = sb("pos", [P, TOPK, NT], i32)
        gate_sb = sb("gate_sb", [P, KD, NE])
        gateb = sb("gateb", [P, NE])
        erow = sb("erow", [1, ST], i32)
        t64 = sb("t64", [1, ST])
        rt = ACC[:, 0:6 * NT * NE].rearrange("p (a t e) -> p a t e", a=6, t=NT)
        small = ACC[:, 6 * NT * NE:6 * NT * NE + 8 * NE].rearrange("p (a e) -> p a e", a=8)
        ecmp = ACC[0:1, 4096:4096 + ST * NE].rearrange("p (t e) -> p t e", t=ST)
        o0 = 0
        def view(n):
            nonlocal o0
            o0 += n
            return ACC[:, o0 - n:o0]
        W1S = view(2 * KD * F).rearrange("p (s k f) -> p s k f", s=2, k=KD)
        W2S = view(2 * KF * D).rearrange("p (s k d) -> p s k d", s=2, k=KF)
        B2S = view(2 * D).rearrange("p (s d) -> p s d", s=2)
        B1S = view(2 * KF).rearrange("p (s k) -> p s k", s=2)
        YS = view(2 * D).rearrange("p (s d) -> p s d", s=2)
        YTS = view(2 * D).rearrange("p (s k n) -> p s k n", s=2, k=KD)
        HTS = view(2 * F).rearrange("p (s k n) -> p s k n", s=2, k=KF)
        OS = view(2 * D).rearrange("p (s d) -> p s d", s=2)
        gam = sb("gam", [P, D])
        bet = sb("bet", [P, D])

        XGf = XG[:, :, :, :].rearrange("p s q d -> p (s q d)")
        RGf = RG[:, :, :, :].rearrange("p s q d -> p (s q d)")
        WC = XGf[:, 0:KD * INNER].rearrange("p (k c) -> p k c", k=KD)
        WX = XGf[:, KD * INNER:2 * KD * INNER].rearrange("p (k c) -> p k c", k=KD)
        WXT = RGf[0:HD, 0:HEADS * D].rearrange("p (h d) -> p h d", h=HEADS)
        WFX = NORM[:, 0:KD * INNER].rearrange("p (k c) -> p k c", k=KD)
        IOf = IOTA[:, :]
        BC = IOf[:, 0:INNER]
        LG = IOf[:, INNER:2 * INNER]
        LG2 = IOf[:, 2 * INNER:3 * INNER]
        EX = IOf[:, 3 * INNER:4 * INNER]
        EX2 = IOf[:, 4 * INNER:5 * INNER]
        bslice = IOf[:, 5 * INNER:5 * INNER + G]
        itemp = IOf[:, 5 * INNER + G:5 * INNER + G + HEADS]
        bxT = IOf[0:HD, 5 * INNER + 128:5 * INNER + 128 + HEADS]
        WOUT = sb("WOUT", [HD, HEADS, D])
        Wsl = sb("Wsl", [HD, G])
        Wqkv = sb("Wqkv", [HD, 3, HD])
        bfx = sb("bfx", [1, INNER])
        mh = sb("mh", [P, 2, HEADS])
        sh = sb("sh", [P, 2, HEADS])
        SN = XGf[:, 0:PAIRS * (D + 1)].rearrange("p (a d) -> p a d", a=PAIRS)
        FTf = FT[:, :, :].rearrange("p k n -> p (k n)")
        VVa = FTf[:, 0:PAIRS * D].rearrange("p (a d) -> p a d", a=PAIRS)
        SNT = FTf[:, 1024:1024 + KD * INNER].rearrange("p (k c) -> p k c", k=KD)
        nrow = FTf[0:1, 2048:2048 + INNER]
        bxB = FTf[0:HD, 2560:2560 + HEADS * P].rearrange("p (h n) -> p h n", h=HEADS)
        SWS = FTf[:, 3584:3584 + PAIRS * CN].rearrange("p (a n) -> p a n", a=PAIRS)
        TKT = RGf[0:HD, 0:INNER]
        QT = RGf[0:HD, INNER:2 * INNER]
        KT = RGf[0:HD, 2 * INNER:3 * INNER]
        VN = RGf[0:HD, 3 * INNER:4 * INNER]
        AT = TNH[0:HD, 0, 0:INNER]
        AE = TNH[0:HD, 1, 0:INNER]
        OST = OH[0:HD, 0, :, :].rearrange("p q n -> p (q n)")
        S1 = sb("S1", [P, 4, 8])
        BOUT = MUB

        tabs = [dram(f"tab{n}", [NPAD, D]) for n in range(4)]
        slot_in = dram("slot_in", [SALL, D])
        slot_out = dram("slot_out", [SALL, D])

        def chunk_rows(t, c):
            return t[ds(c * CN, CN), :].rearrange("(t p) d -> p t d", p=P)

        def wview(w):
            return w.rearrange("(k p) n -> p k n", p=P)

        def bcast(v, parts=P):
            return v.rearrange("(a n) -> a n", a=1).to_broadcast([parts, v.shape[0]])

        block = ctx.enter_context(nc.Block())


        ATT = {"pe": ('wxt', 'wc', 's_done', 'snt', 'tk', 'qkv', 'sc', 'aT', 'os', 'vv'),
               "act": ('wxt_sb', 'snt_sb', 'tk_sb', 'qkv_sb', 'sc_exp', 'aT_sb', 'os_sb', 'vv_sb'),
               "dve": ('bxb_ready', 'wc_sb', 'sn_ready', 'sc_sub', 'at_sb')}

        def att(step):
            for eng, steps in ATT.items():
                if step in steps:
                    return sem("att_" + eng), steps.index(step) + 1

        ROUNDS = NG // SLOTS

        def rounds_before(n):
            return n * ROUNDS

        def rows_before(n):
            return 16 * Q * ROUNDS * (0, 2, 4, 5)[n]


        @block.sync
        def _(sp):
            sp.dma_start(X[:, 0:NT - 1, :], A["x"][0:(NT - 1) * P, :].rearrange("(t p) d -> p t d", p=P)).then_inc(sem("x_loaded"), 16)
            sp.wait_ge(sem("last_tile_zero"), 1)
            sp.dma_start(X[0:LAST, NT - 1, :], A["x"][(NT - 1) * P:N, :]).then_inc(sem("x_loaded"), 16)
            sp.wait_ge(sem("nat_padded"), 3)
            for a, name in enumerate(("dst", "dst", "src", "edge_type_400")):
                for h in range(2):
                    e0, g0 = h * HALF, h * GH
                    full = (GH - 1) * GE
                    sp.dma_start(nat[g0:g0 + GH - 1, a, :], A[name][e0:e0 + full].rearrange("(g e) -> g e", e=GE)).then_inc(sem("edges_loaded"), 16)
                    sp.dma_start(nat[g0 + GH - 1:g0 + GH, a, 0:TAIL], A[name][e0 + full:e0 + HALF].rearrange("(g e) -> g e", g=1)).then_inc(sem("edges_loaded"), 16)
            for n, name in enumerate(("W_in1", "W_out1", "W_loop1")):
                sp.dma_start(WB[:, n], wview(A["L0_gnn_" + name])).then_inc(sem("w_loaded"), 16)
            sp.dma_start(BV[:, :], A["L0_gnn_b1"].rearrange("(k p) -> p k", p=P)).then_inc(sem("w_loaded"), 16)
            sp.dma_start(RES[:, :], bcast(A["L0_gnn_res"])).then_inc(sem("w_loaded"), 16)
            sp.dma_start(MUW[:, :, :], wview(A["L0_gnn_mu_w"])).then_inc(sem("mu_loaded"), 16)
            sp.dma_start(MUB[:, :], bcast(A["L0_gnn_mu_b"])).then_inc(sem("mu_loaded"), 16)
            sp.dma_start(gate_sb[:, :, :], wview(A["L0_ffn_gate_w"])).then_inc(sem("gate_loaded"), 16)
            sp.dma_start(gateb[:, :], bcast(A["L0_ffn_gate_b"])).then_inc(sem("gate_loaded"), 16)
            sp.dma_start(gam[:, :], bcast(A["L0_ffn_gamma"])).then_inc(sem("gate_loaded"), 16)
            sp.dma_start(bet[:, :], bcast(A["L0_ffn_beta"])).then_inc(sem("gate_loaded"), 16)
            sp.dma_start(WOUT[:, :, :], A["L1_ffn_W_out"].rearrange("(h c) d -> c h d", c=HD)).then_inc(sem("att_w"), 16)
            sp.dma_start(Wsl[:, :], A["L1_ffn_W_slice"]).then_inc(sem("att_w"), 16)
            for n, name in enumerate(("W_q", "W_k", "W_v")):
                sp.dma_start(Wqkv[:, n, :], A["L1_ffn_" + name]).then_inc(sem("att_w"), 16)
            sp.dma_start(bfx[:, :], A["L1_ffn_b_fx"].rearrange("(a n) -> a n", a=1)).then_inc(sem("att_w"), 16)
            sp.wait_ge(sem("acc_zero"), 1)
            nz = KD * 2 * AW // D
            sp.dma_start(slot_in[0:nz * P, :].rearrange("(p r) d -> p (r d)", p=P), ACC[:, 0:nz * D]).then_inc(sem("slots_zero"), 16)
            nr = SALL // P - nz
            sp.dma_start(slot_in[nz * P:SALL, :].rearrange("(p r) d -> p (r d)", p=P), ACC[:, 0:nr * D]).then_inc(sem("slots_zero"), 16)
            sp.dma_start(slot_out[SROWS:SALL, :].rearrange("(p r) d -> p (r d)", p=P), ACC[:, 0:2 * D]).then_inc(sem("slots_zero"), 16)

            def store_table(tab, name, ready, credits):
                sp.sem_inc(sem(name + "_nodefree"), 1)
                with sp.Fori(0, CH) as c:
                    sp.wait_ge(sem(ready), c + 1 + credits)
                    sp.dma_start(chunk_rows(tab, c), NODE[:, :, 0:D]).then_inc(sem(name + "_stored"), 16)
                    sp.wait_ge(sem(name + "_stored"), c * 16 + 16)
                    sp.sem_inc(sem(name + "_nodefree"), 1)

            store_table(tabs[0], "t0", "t0_node", 0)
            store_table(tabs[1], "t1", "conv0_zfree", 1)
            sp.wait_ge(sem("conv0_y"), CH)
            for n, name in enumerate(("W_in2", "W_out2", "W_loop2")):
                sp.dma_start(WB[:, n], wview(A["L0_gnn_" + name])).then_inc(sem("w2_loaded"), 16)
            sp.wait_ge(sem("conv0_tanh"), CH + 1)
            sp.dma_start(BV[:, :], A["L0_gnn_b2"].rearrange("(k p) -> p k", p=P)).then_inc(sem("w2_loaded"), 16)

            sp.wait_ge(sem("pos_ready"), 1)
            for s in range(TOPK):
                sp.wait_ge(sem(f"scattered{s}"), 16 * NT)
            with sp.Fori(0, ST // 2) as i:
                for s in range(2):
                    sp.wait_ge(sem(f"ex_free{s}"), i + 1)
                    t = i * 2 + s
                    e = sp.value_load(erow[0:1, ds(t, 1)], min_val=0, max_val=NE - 1)
                    got = sem(f"ex_in{s}")
                    sp.dma_start(YS[:, s, :], slot_in[ds(t * P, P), :]).then_inc(got, 16)
                    sp.dma_start(W1S[:, s], A["L0_ffn_w1"][ds(e, 1)].rearrange("a (k p) f -> p (a k) f", p=P)).then_inc(got, 16)
                    sp.dma_start(W2S[:, s], A["L0_ffn_w2"][ds(e, 1)].rearrange("a (k p) d -> p (a k) d", p=P)).then_inc(got, 16)
                    sp.dma_start(B1S[:, s, :], A["L0_ffn_b1"][ds(e, 1)].rearrange("a (k p) -> p (a k)", p=P)).then_inc(got, 16)
                    sp.dma_start(B2S[:, s, :], A["L0_ffn_b2"][ds(e, 1)].to_broadcast([P, D])).then_inc(got, 16)
            sp.wait_ge(sem("moe_ln"), 1)
            sp.dma_start(WB[:, 0], wview(A["L1_gnn_W1"])).then_inc(sem("w3_loaded"), 16)
            sp.dma_start(WB[:, 1], wview(A["L1_gnn_W2"])).then_inc(sem("w3_loaded"), 16)
            sp.dma_start(gam[:, :], bcast(A["L1_gnn_b1"])).then_inc(sem("w3_loaded"), 16)
            sp.dma_start(bet[:, :], bcast(A["L1_gnn_b2"])).then_inc(sem("w3_loaded"), 16)
            sp.dma_start(BOUT[:, :], bcast(A["L1_ffn_b_out"])).then_inc(sem("w3_loaded"), 16)
            store_table(tabs[2], "t2", "t2_node", 0)
            store_table(tabs[3], "t3", "t3_node", 0)
            sp.wait_ge(sem("pass3_done"), 1)
            sp.dma_start(WX, wview(A["L1_ffn_W_x"])).then_inc(sem("att_w2"), 16)
            sp.dma_start(WFX, wview(A["L1_ffn_W_fx"])).then_inc(sem("att_w2"), 16)
            sp.dma_start(bslice, bcast(A["L1_ffn_b_slice"])).then_inc(sem("att_w2"), 16)
            sp.dma_start(itemp, A["L1_ffn_temperature"].rearrange("a h b c -> a (h b c)").to_broadcast([P, HEADS])).then_inc(sem("att_w2"), 16)
            sp.dma_start(bxT, A["L1_ffn_b_x"].rearrange("(h c) -> c h", c=HD)).then_inc(sem("att_w2"), 16)
            for c in range(CH):
                sp.wait_ge(sem("out_free"), c + 2)
                if c < CH - 1:
                    sp.dma_start(out[c * CN:(c + 1) * CN, :].rearrange("(t p) d -> p t d", p=P), X[:, c * CT:(c + 1) * CT, :]).then_inc(sem("out_stored"), 16)
                else:
                    sp.dma_start(out[c * CN:(NT - 1) * P, :].rearrange("(t p) d -> p t d", p=P), X[:, c * CT:NT - 1, :]).then_inc(sem("out_stored"), 16)
                    sp.dma_start(out[(NT - 1) * P:N, :], X[0:LAST, NT - 1, :]).then_inc(sem("out_stored"), 16)
            sp.wait_ge(sem("out_stored"), 16 * (CH + 1))

        @block.gpsimd
        def _(pool):
            g = nc.gpsimd
            c = sem("pool_chain")
            g.memset(ident[:, :], 0.0).then_inc(c, 1)
            g.memset(ones[:, :], 1.0).then_inc(c, 1)
            g.memset(zeros[:, :], 0.0).then_inc(c, 1)
            g.memset(NODE[:, :, D:D + 1], 1.0).then_inc(c, 1)
            g.memset(rowmask[:, :], 1.0).then_inc(c, 1)
            g.memset(trash[:, 0:NT - 1, :], 0.0).then_inc(c, 1)
            g.iota(IOTA[:, :], pattern=[[1, AW]], base=0, channel_multiplier=0, allow_small_or_imprecise_dtypes=True).then_inc(c, 1)
            g.iota(i16[:, :], pattern=[[1, NE]], base=0, channel_multiplier=0, allow_small_or_imprecise_dtypes=True).then_inc(c, 1)
            g.iota(t64[:, :], pattern=[[P, ST]], base=0, channel_multiplier=0, allow_small_or_imprecise_dtypes=True).then_inc(c, 1)
            g.iota(gpart[:, :], pattern=[[0, 1]], base=0, channel_multiplier=1, allow_small_or_imprecise_dtypes=True).then_inc(c, 1)
            g.iota(trash[:, NT - 1, :], pattern=[[P, TOPK]], base=SROWS, channel_multiplier=1, allow_small_or_imprecise_dtypes=True).then_inc(c, 1)
            pool.wait_ge(c, 11)
            done = sem("const_ready")
            g.affine_select(out=ident[:, :], in_=ident[:, :], compare_op=ALU.not_equal, fill=1.0, base=0, pattern=[[-1, P]], channel_multiplier=1).then_inc(done, 1)
            g.affine_select(out=tri[:, :], in_=ones[:, :], compare_op=ALU.is_gt, fill=0.0, base=0, pattern=[[1, P]], channel_multiplier=-1).then_inc(done, 1)
            g.affine_select(out=rowmask[:, :], in_=rowmask[:, :], compare_op=ALU.is_gt, fill=0.0, base=N, pattern=[[-P, NT]], channel_multiplier=-1).then_inc(done, 1)
            g.affine_select(out=trash[:, :, :], in_=trash[:, :, :], compare_op=ALU.is_ge, fill=0.0, base=-N, pattern=[[P, NT], [0, TOPK]], channel_multiplier=1).then_inc(done, 1)

            def gather_pass(n, tab, stored, rel):
                pool.wait_ge(sem(stored), 16 * CH)
                with pool.Fori(0, NG // SLOTS) as i:
                    for s in range(SLOTS):
                        pool.wait_ge(sem(f"pass_idx{s}"), i + 1 + rounds_before(n))
                        pool.sem_inc(sem("pool_turns"), 1)
                        for q in range(Q):
                            g.indirect_dma_start(out=XG[:, s, q, :], out_offset=None, in_=tab,
                                                 in_offset=bass.IndirectOffsetOnAxis(ap=idx_slot[:, s, q:q + 1], axis=0)).then_inc(sem(f"pass_in{s}"), 16)
                            if rel is not None:
                                g.indirect_dma_start(out=RG[:, s, q, :], out_offset=None, in_=rel,
                                                     in_offset=bass.IndirectOffsetOnAxis(ap=idx_slot[:, s, Q + q:Q + q + 1], axis=0)).then_inc(sem(f"pass_in{s}"), 16)

            gather_pass(0, tabs[0], "t0_stored", A["L0_gnn_rel1"])
            pool.sem_inc(sem("conv0_ft"), 1)
            with pool.Fori(0, CH) as cc:
                pool.wait_ge(sem("conv0_y"), cc + 1)
                for k in range(KD):
                    for h in range(2):
                        last = g.tensor_copy(acc[:, k, ds(cc * CN + h * AW, CN)].rearrange("p (t n) -> p t n", t=CT), zeros[:, None, 0:P].to_broadcast([P, CT, P]))
                last.then_inc(sem("acc_zero1"), 1)
                pool.wait_ge(sem("conv0_h"), cc + 2)
                g.tensor_copy(FT[:, :, ds(cc * CN, CN)], STG[:, :, :]).then_inc(sem("conv0_ft"), 1)
            gather_pass(1, tabs[1], "t1_stored", A["L0_gnn_rel2"])
            with pool.Fori(0, CH) as cc:
                pool.wait_ge(sem("gt_node"), cc + 1)
                g.tensor_copy(FTn[:, ds(cc * CT, CT), :], NODE[:, :, 0:D]).then_inc(sem("gt_copied"), 1)
            pool.wait_ge(sem("gt_copied"), CH)
            pool.wait_ge(sem("slots_zero"), 48)
            pool.wait_ge(sem("pos_ready"), 1)
            for j in range(NT):
                for s in range(TOPK):
                    g.indirect_dma_start(out=slot_in, out_offset=bass.IndirectOffsetOnAxis(ap=pos[:, s, j:j + 1], axis=0),
                                         in_=FTn[:, j, :], in_offset=None).then_inc(sem(f"scattered{s}"), 16)
            g.tensor_tensor(X[:, :, :], X[:, :, :], bet[:, None, :].to_broadcast([P, NT, D]), ALU.add).then_inc(sem("beta_added"), 1)
            for s in range(2):
                pool.wait_ge(sem(f"ex_stored{s}"), 16 * (ST // 2) + 16)
            for j in range(NT):
                for s in range(TOPK):
                    g.indirect_dma_start(out=RR[:, s, j, :], out_offset=None, in_=slot_out,
                                         in_offset=bass.IndirectOffsetOnAxis(ap=pos[:, s, j:j + 1], axis=0)).then_inc(sem(f"moe_in{j // CT}"), 16)
            gather_pass(2, tabs[2], "t2_stored", None)
            gather_pass(3, tabs[3], "t3_stored", None)
            pool.wait_ge(sem("z_node"), CH)
            pool.wait_ge(sem("w3_loaded"), 80)
            g.tensor_tensor(X[:, :, :], X[:, :, :], BOUT[:, None, :].to_broadcast([P, NT, D]), ALU.add).then_inc(sem("bout_added"), 1)

        def pool_tokens(pe, t, j, n):
            pe.wait_ge(sem("z_sw"), n)
            buf = (EX, EX2)[j % 2]
            for a in range(PAIRS):
                t.matmul(bank[a][:, 0:D + 1], buf[:, a * P:(a + 1) * P], NODE[:, j, :], start=False, stop=False)
            pe.wait_ge(sem("z_swt"), n)
            for a in range(PAIRS):
                last = t.transpose(bank[7][:, a * P:(a + 1) * P], buf[:, a * P:(a + 1) * P], ident[:, :])
            last.then_inc(sem("z_swT"), 1)

        @block.tensor
        def _(pe):
            t = nc.tensor
            pe.wait_ge(sem("const_ready"), 4)
            pe.wait_ge(sem("natf_ready"), 1)
            for b, a in enumerate((1, 2, 3)):
                for q in range(Q):
                    last = t.transpose(bank[b][:, q * NG:(q + 1) * NG], natf[:, a, q * P:(q + 1) * P], ident[0:NG, 0:NG])
            last.then_inc(sem("edges_T"), 1)
            pe.wait_ge(sem("grp_ready"), 1)
            for a in range(3):
                last = t.transpose(bank[3][0:1, a * NG:(a + 1) * NG], grp[0:NG, a:a + 1], ident[0:NG, 0:NG])
            last.then_inc(sem("grp_T"), 1)

            def node_T(name, width_sem):
                with pe.Fori(0, CH) as c:
                    pe.wait_ge(sem(name + "_node"), c + 1)
                    pe.wait_ge(sem(name + "_Tfree"), c + 1)
                    for j in range(CT):
                        for k in range(KD):
                            last = t.transpose(bank[4 + j // 2][:, (j % 2) * D + k * P:(j % 2) * D + (k + 1) * P],
                                               NODE[:, j, k * P:(k + 1) * P], ident[:, :])
                    last.then_inc(sem(name + "_T"), 1)

            def sum_pass(n, rel, deg):
                with pe.Fori(0, NG // SLOTS) as i:
                    for s in range(SLOTS):
                        extra = pe.value_load(rows_i[0:1, ds(i * SLOTS + s, 1), 2:3], min_val=0, max_val=NT)
                        pe.wait_ge(sem(f"pass_oh{s}"), i + 1 + rounds_before(n))
                        if rel:
                            pe.wait_ge(sem(f"pass_m{s}"), i + 1 + rounds_before(n))
                        else:
                            pe.wait_ge(sem(f"pass_in{s}"), i * (16 * Q) + 16 * Q + rows_before(n))
                        window(bank[s], s, OH[:, s], deg).then_inc(sem(f"pass_ps{s}"), 1)
                        with pe.If(extra > 0):
                            before = pe.value_load(rows_i[0:1, ds(i * SLOTS + s, 1), 3:4], min_val=0, max_val=NG * NT)
                            with pe.Fori(0, extra) as w:
                                pe.wait_ge(sem(f"p{n}_xoh"), before + w + 1)
                                window(bank[2], s, OHX, deg).then_inc(sem(f"p{n}_xps"), 1)
                        with pe.Else():
                            pe.nop()

            def window(ps, s, oh, deg):
                for k in range(KD):
                    for q in range(Q):
                        last = t.matmul(ps[:, k * P:(k + 1) * P], XG[:, s, q, k * P:(k + 1) * P], oh[:, q, :], start=q == 0, stop=q == Q - 1)
                if deg:
                    for q in range(Q):
                        last = t.matmul(ps[:, KD * P:(KD + 1) * P], ones[:, :], oh[:, q, :], start=q == 0, stop=q == Q - 1)
                return last

            node_T("t0", None)
            pe.wait_ge(sem("rows_ready"), 1)
            sum_pass(0, True, True)
            pe.wait_ge(sem("deg_ready"), 1)
            for j in range(NT):
                last = t.matmul(bank[7][:, j:j + 1], NORM[0:1, j * P:(j + 1) * P], ones[0:1, 0:1], start=True, stop=True)
            last.then_inc(sem("deg_T"), 1)
            for layer in range(2):
                pe.wait_ge(sem("w_loaded" if layer == 0 else "w2_loaded"), 80 if layer == 0 else 64)
                if layer == 1:
                    pe.wait_ge(sem("mu_loaded"), 32)
                with pe.Fori(0, CH) as c:
                    pe.wait_ge(sem(f"conv{layer}_scaled"), c + 1)
                    pe.wait_ge(sem(f"conv{layer}_tanh"), c + 1)
                    for o in range(KD):
                        for b in range(2):
                            at = c * CN + b * CB
                            for n, src in enumerate((acc[:, :, 0:AW], acc[:, :, AW:2 * AW], FT[:, :, :])):
                                for k in range(KD):
                                    last = t.matmul(bank[o * 2 + b][:, 0:CB], WB[:, n, k, o * P:(o + 1) * P], src[:, k, ds(at, CB)],
                                                    start=n + k == 0, stop=n == 2 and k == KD - 1)
                    last.then_inc(sem(f"conv{layer}_y"), 1)
                    pe.wait_ge(sem(f"conv{layer}_h"), c + 2)
                    pe.wait_ge(sem(f"conv{layer}_zfree"), c + 1)
                    for j in range(CT):
                        for k in range(KD):
                            to = bank[4 + j // 2]
                            src = STG[:, k, j * P:(j + 1) * P]
                            if layer == 0:
                                last = t.transpose(to[:, (j % 2) * D + k * P:(j % 2) * D + (k + 1) * P], src, ident[:, :])
                            else:
                                last = t.matmul(to[:, (j % 2) * D:(j % 2 + 1) * D], src, MUW[:, k, :], start=k == 0, stop=k == KD - 1)
                    last.then_inc(sem(f"conv{layer}_z"), 1)
                if layer == 0:
                    sum_pass(1, True, False)
            pe.wait_ge(sem("gate_loaded"), 64)
            with pe.Fori(0, CH) as c:
                pe.wait_ge(sem("gt_node"), c + 1)
                for j in range(CT):
                    for k in range(KD):
                        last = t.transpose(bank[4 + j // 2][:, (j % 2) * D + k * P:(j % 2) * D + (k + 1) * P],
                                           NODE[:, j, k * P:(k + 1) * P], ident[:, :])
                last.then_inc(sem("gt_T"), 1)
                pe.wait_ge(sem("gt_stg"), c + 1)
                for j in range(CT):
                    for k in range(KD):
                        last = t.matmul(bank[0][:, j * NE:(j + 1) * NE], STG[:, k, j * P:(j + 1) * P], gate_sb[:, k, :], start=k == 0, stop=k == KD - 1)
                last.then_inc(sem("gt_log"), 1)
            pe.wait_ge(sem("picks_ready"), 1)
            M = rt[:, 2].rearrange("p t e -> p (t e)")
            t.matmul(bank[1][:, 0:NT * NE], tri[:, :], M, start=True, stop=True)
            t.matmul(bank[2][:, 0:NT * NE], ones[:, :], M, start=True, stop=True).then_inc(sem("ranks"), 1)
            with pe.Fori(0, ST // 2) as i:
                for s in range(2):
                    pe.wait_ge(sem(f"ex_in{s}"), i * 80 + 80)
                    for k in range(KD):
                        last = t.transpose(bank[s][:, k * P:(k + 1) * P], YS[:, s, k * P:(k + 1) * P], ident[:, :])
                    last.then_inc(sem(f"ex_T{s}"), 1)
                for s in range(2):
                    pe.wait_ge(sem(f"ex_yt{s}"), i + 1)
                    for f in range(KF):
                        for k in range(KD):
                            last = t.matmul(bank[2 + s][:, f * P:(f + 1) * P], W1S[:, s, k, f * P:(f + 1) * P], YTS[:, s, k, :], start=k == 0, stop=k == KD - 1)
                    last.then_inc(sem(f"ex_h{s}"), 1)
                for s in range(2):
                    pe.wait_ge(sem(f"ex_ht{s}"), i + 1)
                    for f in range(KF):
                        last = t.matmul(bank[4 + s][:, 0:D], HTS[:, s, f, :], W2S[:, s, f, :], start=f == 0, stop=f == KF - 1)
                    last.then_inc(sem(f"ex_o{s}"), 1)
            for n in (2, 3):
                node_T(f"t{n}", None)
                sum_pass(n, False, False)
                pe.wait_ge(sem("w3_loaded"), 80)
                with pe.Fori(0, CH) as c:
                    pe.wait_ge(sem("g_stg"), c + 1 + (n - 2) * CH)
                    pe.wait_ge(sem("g_free"), c + 1 + (n - 2) * (CH + 1))
                    for j in range(CT):
                        for k in range(KD):
                            last = t.matmul(bank[4 + j // 2][:, (j % 2) * D:(j % 2 + 1) * D], STG[:, k, j * P:(j + 1) * P], WB[:, n - 2, k, :], start=k == 0, stop=k == KD - 1)
                    last.then_inc(sem("g_y"), 1)
            pe.wait_ge(sem("att_w"), 96)
            pe.wait_ge(sem("att_w2"), 80)
            for h in range(HEADS):
                for k in range(KD):
                    last = t.transpose(bank[h // 2][0:HD, (h % 2) * D + k * P:(h % 2) * D + (k + 1) * P], WX[:, k, h * HD:(h + 1) * HD], ident[:, :])
            last.then_inc(att("wxt")[0], 1)
            pe.wait_ge(*att("wxt_sb"))
            for k in range(KD):
                for h in range(HEADS):
                    last = t.matmul(bank[4 + k][:, h * G:(h + 1) * G], WXT[:, h, k * P:(k + 1) * P], Wsl[:, :], start=True, stop=True)
            for h in range(HEADS):
                last = t.matmul(bank[6][:, h * G:(h + 1) * G], bxB[:, h, :], Wsl[:, :], start=True, stop=True)
            last.then_inc(att("wc")[0], 1)
            pe.wait_ge(*att("wc_sb"))
            for a in range(PAIRS):
                t.matmul(bank[a][:, 0:D + 1], zeros[:, 0:P], zeros[:, :], start=True, stop=False)
            with pe.Fori(0, CH) as c:
                pe.wait_ge(sem("z_node"), c + 1)
                for j in range(CT):
                    n = c * CT + j
                    for k in range(KD):
                        last = t.transpose(bank[4][:, k * P:(k + 1) * P], NODE[:, j, k * P:(k + 1) * P], ident[:, :])
                    last.then_inc(sem("z_T"), 1)
                    pe.wait_ge(sem("z_stg"), n + 1)
                    for k in range(KD):
                        last = t.matmul(bank[5 + j % 2][:, :], STG[:, k, j * P:(j + 1) * P], WC[:, k, :], start=k == 0, stop=k == KD - 1)
                    last.then_inc(sem("z_log"), 1)
                    if j:
                        pool_tokens(pe, t, j - 1, n)
                pool_tokens(pe, t, CT - 1, c * CT + CT)
            for a in range(PAIRS):
                last = t.matmul(bank[a][:, 0:D + 1], zeros[:, 0:P], zeros[:, :], start=False, stop=True)
            last.then_inc(att("s_done")[0], 1)
            pe.wait_ge(*att("sn_ready"))
            for k in range(KD):
                for a in range(PAIRS):
                    t.transpose(bank[4 + k][:, a * P:(a + 1) * P], SN[:, a, k * P:(k + 1) * P], ident[:, :])
            for a in range(PAIRS):
                last = t.transpose(bank[6][0:1, a * P:(a + 1) * P], SN[:, a, D:D + 1], ident[:, :])
            last.then_inc(att("snt")[0], 1)
            pe.wait_ge(*att("snt_sb"))
            for h in range(HEADS):
                hs = slice(h * HD, (h + 1) * HD)
                for k in range(KD):
                    t.matmul(bank[0][0:HD, hs], WFX[:, k, hs], SNT[:, k, hs], start=k == 0, stop=False)
                last = t.matmul(bank[0][0:HD, hs], bfx[0:1, hs], nrow[0:1, hs], start=False, stop=True)
            last.then_inc(att("tk")[0], 1)
            pe.wait_ge(*att("tk_sb"))
            t.matmul(bank[1][0:HD, :], Wqkv[:, 0, :], TKT, start=True, stop=True)
            t.matmul(bank[2][0:HD, :], Wqkv[:, 1, :], TKT, start=True, stop=True)
            for h in range(HEADS):
                hs = slice(h * HD, (h + 1) * HD)
                last = t.matmul(bank[3][0:HD, hs], TKT[:, hs], Wqkv[:, 2, :], start=True, stop=True)
            last.then_inc(att("qkv")[0], 1)
            pe.wait_ge(*att("qkv_sb"))
            for h in range(HEADS):
                hs = slice(h * HD, (h + 1) * HD)
                last = t.matmul(bank[0][0:HD, hs], QT[:, hs], KT[:, hs], start=True, stop=True)
            last.then_inc(att("sc")[0], 1)
            pe.wait_ge(*att("at_sb"))
            for h in range(HEADS):
                hs = slice(h * HD, (h + 1) * HD)
                last = t.transpose(bank[1][0:HD, hs], AT[:, hs], ident[0:HD, 0:HD])
            last.then_inc(att("aT")[0], 1)
            pe.wait_ge(*att("aT_sb"))
            for h in range(HEADS):
                hs = slice(h * HD, (h + 1) * HD)
                last = t.matmul(bank[2][0:HD, hs], VN[:, hs], AE[:, hs], start=True, stop=True)
            last.then_inc(att("os")[0], 1)
            pe.wait_ge(*att("os_sb"))
            for a in range(PAIRS):
                for b in range(2):
                    last = t.matmul(bank[4 + a][:, b * D:(b + 1) * D], OST[:, a * P:(a + 1) * P], WOUT[:, 2 * a + b, :], start=True, stop=True)
            last.then_inc(att("vv")[0], 1)
            pe.wait_ge(*att("vv_sb"))
            with pe.Fori(0, CH) as c:
                pe.wait_ge(sem("sw_stg"), c + 1)
                pe.wait_ge(sem("out_free"), c + 1)
                for j in range(CT):
                    for a in range(PAIRS):
                        last = t.matmul(bank[j // 2][:, (j % 2) * D:(j % 2 + 1) * D], SWS[:, a, j * P:(j + 1) * P], VVa[:, a, :], start=a == 0, stop=a == PAIRS - 1)
                last.then_inc(sem("o_done"), 1)

        def copy_swT(act, a_, n, at):
            act.wait_ge(sem("z_swT"), n)
            a_.copy(SWT[:, :, ds(at * P, P)], bank[7][:, :].rearrange("p (a n) -> p a n", a=PAIRS)).then_inc(sem("z_swt"), 1)

        @block.scalar
        def _(act):
            a_ = nc.scalar
            chain = Chain(act, sem("act_chain"))

            def root(n):
                act.wait_ge(sem("var_ready"), n + 1)
                a_.activation(rstd[:, :], rstd[:, :], ACT.Sqrt).then_inc(sem("root_ready"), 1)

            def copy_T(name, to):
                act.sem_inc(sem(name + "_Tfree"), 1)
                with act.Fori(0, CH) as c:
                    act.wait_ge(sem(name + "_T"), c + 1)
                    for b in range(3):
                        w = 2 if b < 2 else 1
                        src = bank[4 + b][:, 0:w * D].rearrange("p (j k n) -> p k j n", j=w, k=KD)
                        last = a_.copy(to[:, :, ds(c * CN + b * 2 * P, w * P)].rearrange("p k (j n) -> p k j n", j=w), src)
                    last.then_inc(sem(name + "_Tfree"), 1)

            def index_pass(n):
                with act.Fori(0, NG // SLOTS) as i:
                    for s in range(SLOTS):
                        act.wait_ge(sem(f"pass_free{s}"), i + 1 + rounds_before(n))
                        a_.copy(idx_slot[:, s, :], idx_all[:, ds(i * SLOTS + s, 1), :].rearrange("p a b -> p (a b)")).then_inc(sem(f"pass_idx{s}"), 1)

            root(0)
            copy_T("t0", FT[:, :, :])
            index_pass(0)
            act.wait_ge(sem("deg1"), 1)
            a_.activation(DINV[:, :], DINV[:, :], ACT.Sqrt).then_inc(sem("deg_root"), 1)
            for layer in range(2):
                act.wait_ge(sem("w_loaded" if layer == 0 else "w2_loaded"), 80 if layer == 0 else 64)
                act.sem_inc(sem(f"conv{layer}_tanh"), 1)
                if layer == 0:
                    act.sem_inc(sem("conv0_zfree"), 1)
                with act.Fori(0, CH) as c:
                    act.wait_ge(sem(f"conv{layer}_y"), c + 1)
                    act.wait_ge(sem(f"conv{layer}_h"), c + 1)
                    for o in range(KD):
                        for b in range(2):
                            last = a_.activation(TNH[:, o, b * CB:(b + 1) * CB], bank[o * 2 + b][:, 0:CB], ACT.Tanh, bias=BV[:, o:o + 1])
                    last.then_inc(sem(f"conv{layer}_tanh"), 1)
                    if layer == 0:
                        act.wait_ge(sem("conv0_z"), c + 1)
                        act.wait_ge(sem("t1_nodefree"), c + 1)
                        for b in range(3):
                            w = 2 if b < 2 else 1
                            last = a_.copy(NODE[:, 2 * b:2 * b + w, 0:D], bank[4 + b][:, 0:w * D].rearrange("p (j d) -> p j d", j=w))
                        last.then_inc(sem("conv0_zfree"), 1)
                if layer == 0:
                    index_pass(1)
            root(1)
            with act.Fori(0, CH) as c:
                act.wait_ge(sem("gt_T"), c + 1)
                for b in range(3):
                    w = 2 if b < 2 else 1
                    src = bank[4 + b][:, 0:w * D].rearrange("p (j k n) -> p k j n", j=w, k=KD)
                    last = a_.copy(STG[:, :, b * 2 * P:(b * 2 + w) * P].rearrange("p k (j n) -> p k j n", j=w), src)
                last.then_inc(sem("gt_stg"), 1)
            act.wait_ge(sem("top_diff"), 1)
            a_.activation(topw[:, :, 1:2], topw[:, :, 1:2], ACT.Exp).then_inc(sem("top_exp"), 1)
            for s in range(2):
                act.sem_inc(sem(f"ex_stored{s}"), 16)
            with act.Fori(0, ST // 2) as i:
                for s in range(2):
                    act.wait_ge(sem(f"ex_T{s}"), i + 1)
                    a_.copy(YTS[:, s], bank[s][:, 0:D].rearrange("p (k n) -> p k n", k=KD)).then_inc(sem(f"ex_yt{s}"), 1)
                for s in range(2):
                    act.wait_ge(sem(f"ex_h{s}"), i + 1)
                    for f in range(KF):
                        last = a_.activation(HTS[:, s, f, :], bank[2 + s][:, f * P:(f + 1) * P], ACT.Relu, bias=B1S[:, s, f:f + 1])
                    last.then_inc(sem(f"ex_ht{s}"), 1)
                for s in range(2):
                    act.wait_ge(sem(f"ex_os{s}"), i + 1)
                    act.dma_start(slot_out[ds((i * 2 + s) * P, P), :], OS[:, s, :]).then_inc(sem(f"ex_stored{s}"), 16)
            root(2)
            root(3)
            for n in (2, 3):
                if n == 3:
                    act.wait_ge(sem("nrm_sq"), 1)
                    a_.activation(tmpn[:, :], tmpn[:, :], ACT.Sqrt).then_inc(sem("nrm_root"), 1)
                copy_T(f"t{n}", acc_self)
                index_pass(n)
                with act.Fori(0, CH) as c:
                    act.wait_ge(sem("g_free"), c + 1 + (n - 2) * (CH + 1))
                    a_.copy(STG[:, :, :], acc_self[:, :, ds(c * CN, CN)]).then_inc(sem("g_stg"), 1)
            root(4)
            act.sem_inc(sem("z_swt"), 1)
            act.wait_ge(*att("wxt"))
            act.wait_ge(*att("bxb_ready"))
            for b in range(PAIRS):
                last = a_.copy(WXT[:, 2 * b:2 * b + 2, :], bank[b][0:HD, :].rearrange("p (h d) -> p h d", h=2))
            last.then_inc(att("wxt_sb")[0], 1)
            with act.Fori(0, CH) as c:
                for j in range(CT):
                    n = c * CT + j
                    act.wait_ge(sem("z_T"), n + 1)
                    a_.copy(STG[:, :, j * P:(j + 1) * P], bank[4][:, 0:D].rearrange("p (k n) -> p k n", k=KD)).then_inc(sem("z_stg"), 1)
                    act.wait_ge(sem("z_lg"), n + 1)
                    a_.activation((EX, EX2)[j % 2], (LG, LG2)[j % 2], ACT.Exp).then_inc(sem("z_ex"), 1)
                    if j:
                        copy_swT(act, a_, n, c * CT + j - 1)
                copy_swT(act, a_, c * CT + CT, c * CT + CT - 1)
            act.wait_ge(*att("snt"))
            for k in range(KD):
                a_.copy(SNT[:, k, :], bank[4 + k][:, :])
            a_.copy(nrow, bank[6][0:1, :]).then_inc(att("snt_sb")[0], 1)
            act.wait_ge(*att("tk"))
            a_.copy(TKT, bank[0][0:HD, :]).then_inc(att("tk_sb")[0], 1)
            act.wait_ge(*att("qkv"))
            a_.copy(QT, bank[1][0:HD, :])
            a_.copy(KT, bank[2][0:HD, :])
            a_.copy(VN, bank[3][0:HD, :]).then_inc(att("qkv_sb")[0], 1)
            act.wait_ge(*att("sc_sub"))
            a_.activation(AT, AT, ACT.Exp, scale=ATT_SCALE).then_inc(att("sc_exp")[0], 1)
            act.wait_ge(*att("aT"))
            a_.copy(AE, bank[1][0:HD, :]).then_inc(att("aT_sb")[0], 1)
            act.wait_ge(*att("os"))
            a_.copy(OST, bank[2][0:HD, :]).then_inc(att("os_sb")[0], 1)
            act.wait_ge(*att("vv"))
            for a in range(PAIRS):
                for b in range(2):
                    last = a_.copy(VVa[b * G:(b + 1) * G, a, :], bank[4 + a][b * G:(b + 1) * G, b * D:(b + 1) * D])
            last.then_inc(att("vv_sb")[0], 1)
            with act.Fori(0, CH) as c:
                act.wait_ge(sem("out_free"), c + 1)
                a_.copy(SWS, SWT[:, :, ds(c * CN, CN)]).then_inc(sem("sw_stg"), 1)

        @block.vector
        def _(dve):
            v = nc.vector
            chain = Chain(dve, sem("dve_chain"))
            v.memset(X[:, NT - 1, :], 0.0).then_inc(sem("last_tile_zero"), 1)
            v.memset(S1[:, :, :], 0.0)
            v.memset(tmpn[:, :], 0.0)
            v.memset(nat[:, 0, :], NPAD).then_inc(sem("nat_padded"), 1)
            v.memset(nat[:, 1, :], -1).then_inc(sem("nat_padded"), 1)
            v.memset(nat[:, 2:4, :], 0).then_inc(sem("nat_padded"), 1)

            def row_stats(src, mv):
                with chain.loop(CH, 1) as c:
                    for j in range(CT):
                        last = (v.bn_stats(stats[:, ds(c * CT + j, 1), :].rearrange("p a b -> p (a b)"), src[:, ds(c * CT + j, 1), :].rearrange("p a b -> p (a b)")))
                    chain(last)
                for j in range(NT):
                    last = v.bn_aggr(mv[:, j, :], stats[:, j, :])
                chain(last)

            def ln_stats(n, src, mask=False):
                row_stats(src, mv)
                v.tensor_scalar(rstd[:, :], mv[:, :, 1], LN_EPS, None, ALU.add).then_inc(sem("var_ready"), 1)
                dve.wait_ge(sem("root_ready"), n + 1)
                chain(v.reciprocal(rstd[:, :], rstd[:, :]))
                if mask:
                    dve.wait_ge(sem("const_ready"), 4)
                    chain(v.tensor_tensor(rstd[:, :], rstd[:, :], rowmask[:, :], ALU.mult))

            def normalised(name, tile):
                with dve.Fori(0, CH) as c:
                    dve.wait_ge(sem(name + "_nodefree"), c + 1)
                    dve.wait_ge(sem(name + "_Tfree"), c + 1)
                    for j in range(CT):
                        last = tile(NODE[:, j, 0:D], c * CT + j)
                    last.then_inc(sem(name + "_node"), 1)

            def at3(x, at):
                return x[:, ds(at, 1), :].rearrange("p a b -> p (a b)")

            def centred(scale):
                def tile(to, at):
                    return v.tensor_scalar(to, at3(X, at), mv[:, ds(at, 1), 0:1].rearrange("p a b -> p (a b)"), scale[:, ds(at, 1)], ALU.subtract, ALU.mult)
                return tile

            dve.wait_ge(sem("edges_loaded"), 256)
            v.tensor_copy(natf, nat).then_inc(sem("natf_ready"), 1)
            dve.wait_ge(sem("natf_ready"), 1)
            dve.wait_ge(sem("const_ready"), 4)
            gs = slice(0, NG)
            chain(v.tensor_reduce(grp[gs, 0:1], natf[:, 0, :], AX, ALU.min))
            chain(v.tensor_reduce(grp[gs, 2:3], natf[:, 1, :], AX, ALU.max))
            chain(v.tensor_scalar(grp[gs, 3:4], gpart[gs, :], float(GH), float(AW), ALU.is_ge, ALU.mult))
            chain(v.tensor_tensor(grp[gs, 1:2], grp[gs, 3:4], grp[gs, 0:1], ALU.add))
            chain(v.tensor_tensor(grp[gs, 2:3], grp[gs, 2:3], grp[gs, 0:1], ALU.subtract))
            v.tensor_scalar(grp[gs, 2:3], grp[gs, 2:3], 1.0 / P, -0.5 + 0.5 / P, ALU.mult, ALU.add).then_inc(sem("grp_ready"), 1)
            dve.wait_ge(sem("edges_T"), 1)
            def by_group(b):
                return bank[b][:, 0:Q * NG].rearrange("p (q g) -> p q g", q=Q)
            v.tensor_copy(dst_all[:, :, :].rearrange("p g q -> p q g"), by_group(0))
            v.tensor_copy(idx_all[:, :, 0:Q].rearrange("p g q -> p q g"), by_group(1))
            v.tensor_copy(idx_all[:, :, Q:2 * Q].rearrange("p g q -> p q g"), by_group(2))
            dve.wait_ge(sem("grp_T"), 1)
            for a in range(3):
                chain(v.tensor_copy(rows_i[:, :, a], bank[3][0:1, a * NG:(a + 1) * NG]))
            chain(v.tensor_copy(grow[:, 0, :], rows_i[:, :, 2]))
            chain(v.memset(grow[:, 1, :], 1.0))
            chain(v.tensor_tensor_scan(grow[:, 2, :], grow[:, 1, :], grow[:, 0, :], 0.0, ALU.mult, ALU.add))
            chain(v.tensor_tensor(grow[:, 3, :], grow[:, 2, :], grow[:, 0, :], ALU.subtract))
            v.tensor_copy(rows_i[:, :, 3], grow[:, 3, :]).then_inc(sem("rows_ready"), 1)
            dve.wait_ge(sem("rows_ready"), 1)
            v.memset(NORM[:, :], 0.0)
            v.memset(ACC[:, :], 0.0).then_inc(sem("acc_zero"), 1)

            dve.wait_ge(sem("x_loaded"), 32)
            ln_stats(0, X)
            normalised("t0", centred(rstd))

            def sum_pass(n, rel, deg):
                if n == 0:
                    for s in range(SLOTS):
                        dve.sem_inc(sem(f"pass_free{s}"), 1)
                dve.sem_inc(sem(f"p{n}_xadd"), 1)
                per = 16 * Q * (2 if rel else 1)
                with dve.Fori(0, NG // SLOTS) as i:
                    for s in range(SLOTS):
                        g = i * SLOTS + s
                        base = dve.value_load(rows_i[0:1, ds(g, 1), 0:1], min_val=0, max_val=NPAD)
                        extra = dve.value_load(rows_i[0:1, ds(g, 1), 2:3], min_val=0, max_val=NT)
                        to = dve.value_load(rows_i[0:1, ds(g, 1), 1:2], min_val=0, max_val=NPAD + AW) if rel else base

                        def onehot(oh, b):
                            return v.tensor_tensor(oh, IOTA[:, None, ds(b, P)].to_broadcast([P, Q, P]),
                                                   dst_all[:, ds(g, 1), :].rearrange("p a q -> p q a").to_broadcast([P, Q, P]), ALU.is_equal)

                        def add(ps, at, dg):
                            if deg:
                                v.tensor_tensor(NORM[:, ds(dg, P)], NORM[:, ds(dg, P)], ps[:, KD * P:(KD + 1) * P], ALU.add)
                            return v.tensor_tensor(acc[:, :, ds(at, P)], acc[:, :, ds(at, P)],
                                                   ps[:, 0:KD * P].rearrange("p (k n) -> p k n", k=KD), ALU.add)

                        onehot(OH[:, s], base).then_inc(sem(f"pass_oh{s}"), 1)
                        dve.wait_ge(sem(f"pass_in{s}"), i * per + per + rows_before(n))
                        if rel:
                            v.tensor_tensor(XG[:, s], XG[:, s], RG[:, s], ALU.mult).then_inc(sem(f"pass_m{s}"), 1)
                        if s == 0:
                            dve.wait_ge(sem(f"pass_free{SLOTS - 1}"), i + 1 + rounds_before(n))
                        else:
                            dve.wait_ge(sem(f"pass_free{s - 1}"), i + 2 + rounds_before(n))
                        dve.sem_inc(sem("dve_turns"), 1)
                        with dve.If(extra > 0):
                            before = dve.value_load(rows_i[0:1, ds(g, 1), 3:4], min_val=0, max_val=NG * NT)
                            with dve.Fori(0, extra) as w:
                                xbase = nc.s_assert_within(base + w * P + P, 0, NPAD, skip_runtime_bounds_check_because="the window starts at a node")
                                xto = nc.s_assert_within(to + w * P + P, 0, NPAD + AW, skip_runtime_bounds_check_because="the window starts at a node") if rel else xbase
                                onehot(OHX[:, :, :], xbase).then_inc(sem(f"p{n}_xoh"), 1)
                                dve.wait_ge(sem(f"p{n}_xps"), before + w + 1)
                                add(bank[2], xto, xbase).then_inc(sem(f"p{n}_xadd"), 1)
                                dve.wait_ge(sem(f"p{n}_xadd"), before + w + 2)
                                dve.sem_inc(sem("dve_turns"), 1)
                        with dve.Else():
                            dve.nop()
                        dve.wait_ge(sem(f"pass_ps{s}"), i + 1 + rounds_before(n))
                        add(bank[s], to, base).then_inc(sem(f"pass_free{s}"), 1)
                for s in range(SLOTS):
                    dve.wait_ge(sem(f"pass_free{s}"), ROUNDS + 1 + rounds_before(n))

            sum_pass(0, True, True)
            dve.sem_inc(sem("deg_ready"), 1)
            dve.wait_ge(sem("deg_T"), 1)
            v.tensor_scalar(DINV[:, :], bank[7][:, 0:NT], 1.0, None, ALU.add).then_inc(sem("deg1"), 1)
            dve.wait_ge(sem("deg_root"), 1)
            chain(v.reciprocal(DINV[:, :], DINV[:, :]))
            chain(v.tensor_scalar(NORM[:, 0:NPAD], NORM[:, 0:NPAD], 1.0, None, ALU.max))
            chain(v.reciprocal(NORM[:, 0:NPAD], NORM[:, 0:NPAD]))
            for layer in range(2):
                with dve.Fori(0, CH) as c:
                    for k in range(KD):
                        for h in range(2):
                            part = acc[:, k, ds(c * CN + h * AW, CN)]
                            last = v.tensor_tensor(part, part, NORM[:, ds(c * CN, CN)], ALU.mult)
                    last.then_inc(sem(f"conv{layer}_scaled"), 1)
                dve.sem_inc(sem(f"conv{layer}_h"), 1)
                if layer == 0:
                    dve.wait_ge(sem("w_loaded"), 80)
                else:
                    dve.sem_inc(sem("conv1_zfree"), 1)
                    dve.wait_ge(sem("conv0_ft"), CH + 1)
                with dve.Fori(0, CH) as c:
                    dve.wait_ge(sem(f"conv{layer}_tanh"), c + 2)
                    dve.wait_ge(sem(f"conv{layer}_zfree"), c + 1)
                    if layer == 0:
                        dve.wait_ge(sem("conv0_ft"), c + 1)
                    v.scalar_tensor_tensor(STG[:, :, :], TNH[:, :, :], RES[:, 0:1], FT[:, :, ds(c * CN, CN)], ALU.mult, ALU.add).then_inc(sem(f"conv{layer}_h"), 1)
                    if layer == 1:
                        dve.wait_ge(sem("conv1_z"), c + 1)
                        for b in range(3):
                            w = 2 if b < 2 else 1
                            part = X[:, ds(c * CT + 2 * b, w), :]
                            last = v.tensor_tensor(part, part, bank[4 + b][:, 0:w * D].rearrange("p (j d) -> p j d", j=w), ALU.add)
                        last.then_inc(sem("conv1_zfree"), 1)
                if layer == 0:
                    dve.wait_ge(sem("mu_loaded"), 32)
                    chain(v.tensor_tensor(X[:, :, :], X[:, :, :], MUB[:, None, :].to_broadcast([P, NT, D]), ALU.add))
                    dve.wait_ge(sem("acc_zero1"), CH)
                    sum_pass(1, True, False)
                else:
                    dve.wait_ge(sem("conv1_zfree"), CH + 1)

            ln_stats(1, X)
            dve.wait_ge(sem("gate_loaded"), 64)
            with dve.Fori(0, CH) as c:
                for j in range(CT):
                    last = centred(rstd)(NODE[:, j, 0:D], c * CT + j)
                last.then_inc(sem("gt_node"), 1)
                dve.wait_ge(sem("gt_log"), c + 1)
                dve.wait_ge(sem("gt_copied"), c + 1)
                v.tensor_tensor(LOG[:, ds(c * CT, CT), :], bank[0][:, 0:CT * NE].rearrange("p (j e) -> p j e", j=CT), gateb[:, None, :].to_broadcast([P, CT, NE]), ALU.add).then_inc(sem("log_ready"), 1)
            dve.wait_ge(sem("log_ready"), CH)
            for j in range(NT):
                last = v.max(mx8[:, j, :], LOG[:, j, :])
            chain(last)
            for j in range(NT):
                last = v.max_index(mi8[:, j, :], mx8[:, j, :], LOG[:, j, :])
            chain(last)
            v.tensor_tensor(topw[:, :, 1], mx8[:, :, 1], mx8[:, :, 0], ALU.subtract).then_inc(sem("top_diff"), 1)
            chain(v.tensor_copy(topf[:, :, :], mi8[:, :, 0:TOPK]))
            dve.wait_ge(sem("top_exp"), 1)
            chain(v.tensor_scalar(topw[:, :, 0], topw[:, :, 1], 1.0, None, ALU.add))
            chain(v.reciprocal(topw[:, :, 0], topw[:, :, 0]))
            chain(v.tensor_tensor(topw[:, :, 1], topw[:, :, 1], topw[:, :, 0], ALU.mult))
            wide = [P, NT, NE]
            for s in range(TOPK):
                chain(v.tensor_tensor(rt[:, s], i16[:, None, :].to_broadcast(wide), topf[:, :, s:s + 1].to_broadcast(wide), ALU.is_equal))
                chain(v.tensor_tensor(rt[:, s], rt[:, s], rowmask[:, :, None].to_broadcast(wide), ALU.mult))
            v.tensor_tensor(rt[:, 2], rt[:, 0], rt[:, 1], ALU.add).then_inc(sem("picks_ready"), 1)
            dve.wait_ge(sem("ranks"), 1)
            chain(v.tensor_copy(rt[:, 3], bank[2][:, 0:NT * NE].rearrange("p (t e) -> p t e", t=NT)))
            cur, nxt, d = 3, 4, 1
            while d < NT:
                chain(v.tensor_copy(rt[:, nxt, 0:d, :], rt[:, cur, 0:d, :]))
                chain(v.tensor_tensor(rt[:, nxt, d:NT, :], rt[:, cur, d:NT, :], rt[:, cur, 0:NT - d, :], ALU.add))
                cur, nxt, d = nxt, cur, 2 * d
            small_i = small.bitcast(i32)
            chain(v.tensor_scalar(small_i[:, 1, :], rt[:, cur, NT - 1, :], 1.0 / P, 0.5 - 0.5 / P, ALU.mult, ALU.add))
            chain(v.tensor_scalar(small[:, 2, :], small_i[:, 1, :], float(P), None, ALU.mult))
            chain(v.memset(small[:, 4, :], 1.0))
            chain(v.tensor_tensor_scan(small[:, 3, :], small[:, 4, :], small[:, 2, :], 0.0, ALU.mult, ALU.add))
            chain(v.tensor_tensor(small[:, 5, :], small[:, 3, :], small[:, 2, :], ALU.subtract))
            chain(v.tensor_tensor(rt[:, cur], rt[:, cur], bank[2][:, 0:NT * NE].rearrange("p (t e) -> p t e", t=NT), ALU.subtract))
            chain(v.tensor_tensor(rt[:, cur], rt[:, cur], bank[1][:, 0:NT * NE].rearrange("p (t e) -> p t e", t=NT), ALU.add))
            chain(v.tensor_tensor(rt[:, cur], rt[:, cur], small[:, 5:6, :].to_broadcast(wide), ALU.add))
            for s in range(TOPK):
                chain(v.tensor_tensor(rt[:, s], rt[:, s], rt[:, cur], ALU.mult))
                chain(v.tensor_reduce(tmpn[:, :], rt[:, s], AX, ALU.add))
                chain(v.tensor_tensor(pos[:, s, :], tmpn[:, :], trash[:, :, s], ALU.add))
            chain(v.tensor_tensor(ecmp, t64[:, :, None].to_broadcast([1, ST, NE]), small[0:1, 3:4, :].to_broadcast([1, ST, NE]), ALU.is_ge))
            chain(v.tensor_reduce(t64[:, :], ecmp, AX, ALU.add))
            chain(v.tensor_scalar(erow[:, :], t64[:, :], NE - 1.0, None, ALU.min))
            dve.sem_inc(sem("pos_ready"), 1)
            for s in range(2):
                dve.sem_inc(sem(f"ex_free{s}"), 1)
            with dve.Fori(0, ST // 2) as i:
                for s in range(2):
                    dve.wait_ge(sem(f"ex_o{s}"), i + 1)
                    dve.wait_ge(sem(f"ex_stored{s}"), i * 16 + 16)
                    v.tensor_tensor(OS[:, s, :], bank[4 + s][:, 0:D], B2S[:, s, :], ALU.add).then_inc(sem(f"ex_os{s}"), 1)
                    dve.wait_ge(sem(f"ex_os{s}"), i + 1)
                    dve.sem_inc(sem(f"ex_free{s}"), 1)
            for c in range(CH):
                dve.wait_ge(sem(f"moe_in{c}"), 16 * TOPK * CT)
                for s in range(TOPK):
                    for j in range(c * CT, c * CT + CT):
                        last = v.scalar_tensor_tensor(FTn[:, j, :], RR[:, s, j, :], topw[:, j, s:s + 1], FTn[:, j, :], ALU.mult, ALU.add)
                    chain(last)
            ln_stats(2, FTn)
            dve.wait_ge(sem("beta_added"), 1)
            for k in range(2):
                with chain.loop(CH, 1) as c:
                    for j in range(CT):
                        at = c * CT + j
                        y = at3(FTn, at)
                        if k == 0:
                            last = v.scalar_tensor_tensor(y, y, mv[:, ds(at, 1), 0:1].rearrange("p a b -> p (a b)"), gam[:, :], ALU.subtract, ALU.mult)
                        else:
                            last = v.scalar_tensor_tensor(at3(X, at), y, rstd[:, ds(at, 1)], at3(X, at), ALU.mult, ALU.add)
                    chain(last)
            dve.sem_inc(sem("moe_ln"), 1)

            ln_stats(3, X)
            chain(v.tensor_tensor(tmpn[:, :], rstd[:, :], DINV[:, :], ALU.mult))
            normalised("t2", centred(tmpn))
            for n in (2, 3):
                dve.wait_ge(sem(f"t{n}_Tfree"), CH + 1)
                sum_pass(n, False, False)
                dve.wait_ge(sem("w3_loaded"), 80)
                dve.sem_inc(sem("g_free"), 1)
                with dve.Fori(0, CH) as c:
                    dve.wait_ge(sem("g_y"), c + 1 + (n - 2) * CH)
                    for j in range(CT):
                        at = c * CT + j
                        y = bank[4 + j // 2][:, (j % 2) * D:(j % 2 + 1) * D]
                        if n == 2:
                            last = v.scalar_tensor_tensor(at3(FTn, at), y, DINV[:, ds(at, 1)], gam[:, :], ALU.mult, ALU.add)
                        else:
                            last = v.scalar_tensor_tensor(at3(X, at), y, DINV[:, ds(at, 1)], at3(X, at), ALU.mult, ALU.add)
                    last.then_inc(sem("g_free"), 1)
                dve.wait_ge(sem("g_free"), (n - 1) * (CH + 1))
                if n == 2:
                    row_stats(FTn, mv2)
                    chain(v.tensor_tensor(tmpn[:, :], mv2[:, :, 0], mv2[:, :, 0], ALU.mult))
                    chain(v.tensor_tensor(tmpn[:, :], tmpn[:, :], mv2[:, :, 1], ALU.add))
                    v.tensor_scalar(tmpn[:, :], tmpn[:, :], float(D), None, ALU.mult).then_inc(sem("nrm_sq"), 1)
                    dve.wait_ge(sem("nrm_root"), 1)
                    chain(v.tensor_scalar(tmpn[:, :], tmpn[:, :], 1e-12, None, ALU.max))
                    chain(v.reciprocal(tmpn[:, :], tmpn[:, :]))
                    chain(v.tensor_tensor(tmpn[:, :], tmpn[:, :], DINV[:, :], ALU.mult))
                    normalised("t3", lambda to, at: v.tensor_scalar(to, at3(FTn, at), tmpn[:, ds(at, 1)], None, ALU.mult))
                    chain(v.tensor_tensor(shift[:, :], mv[:, :, 0], rstd[:, :], ALU.mult))
                    chain(v.tensor_scalar(rstd[:, :], rstd[:, :], 1.0, None, ALU.add))
                    with chain.loop(CH, 1) as c:
                        for j in range(CT):
                            at = c * CT + j
                            last = v.tensor_scalar(at3(X, at), at3(X, at), rstd[:, ds(at, 1)], shift[:, ds(at, 1)], ALU.mult, ALU.subtract)
                        chain(last)
                    chain(v.tensor_tensor(X[:, :, :], X[:, :, :], bet[:, None, :].to_broadcast([P, NT, D]), ALU.add))
            dve.sem_inc(sem("pass3_done"), 1)

            ln_stats(4, X, mask=True)
            dve.wait_ge(sem("att_w2"), 80)
            chain(v.tensor_scalar(itemp, itemp, 0.1, 5.0, ALU.max, ALU.min))
            chain(v.reciprocal(itemp, itemp))
            v.tensor_copy(bxB, bxT[:, :, None].to_broadcast([HD, HEADS, P])).then_inc(att("bxb_ready")[0], 1)
            dve.wait_ge(*att("wc"))
            hg = [P, HEADS, G]
            def heads(x):
                return x.rearrange("p (h g) -> p h g", h=HEADS)
            it = itemp[:, :, None].to_broadcast(hg)
            for k in range(KD):
                chain(v.tensor_tensor(heads(WC[:, k, :]), heads(bank[4 + k][:, :]), it, ALU.mult))
            chain(v.tensor_tensor(heads(BC), heads(bank[6][:, :]), bslice[:, None, :].to_broadcast(hg), ALU.add))
            v.tensor_tensor(heads(BC), heads(BC), it, ALU.mult).then_inc(att("wc_sb")[0], 1)
            dve.wait_ge(*att("wc_sb"))
            with chain.loop(CH, 5 * CT) as c:
                dve.wait_ge(sem("z_swt"), c * CT + 1)
                v.tensor_copy(NODE[:, :, D:D + 1], rowmask[:, ds(c * CT, CT)][:, :, None])
                for j in range(CT):
                    last = centred(rstd)(NODE[:, j, 0:D], c * CT + j)
                last.then_inc(sem("z_node"), 1)
                for j in range(CT):
                    n = c * CT + j
                    lg, ex = (LG, LG2)[j % 2], (EX, EX2)[j % 2]
                    m, s_ = mh[:, j % 2, :], sh[:, j % 2, :]
                    dve.wait_ge(sem("z_log"), n + 1)
                    chain(v.tensor_tensor(lg, bank[5 + j % 2][:, :], BC, ALU.add))
                    chain(v.tensor_reduce(m, heads(lg), AX, ALU.max))
                    v.tensor_tensor(heads(lg), heads(lg), m[:, :, None].to_broadcast(hg), ALU.subtract).then_inc(sem("z_lg"), 1)
                    dve.wait_ge(sem("z_ex"), n + 1)
                    chain(v.tensor_reduce(s_, heads(ex), AX, ALU.add))
                    chain(v.reciprocal(s_, s_))
                    chain(v.tensor_tensor(heads(ex), heads(ex), s_[:, :, None].to_broadcast(hg), ALU.mult))
                    dve.sem_inc(sem("z_sw"), 1)
            dve.wait_ge(*att("s_done"))
            for a in range(PAIRS):
                chain(v.tensor_scalar(S1[:, a, 0:1], bank[a][:, D:D + 1], TOKEN_EPS, None, ALU.add))
                chain(v.reciprocal(S1[:, a, 1:2], S1[:, a, 0:1]))
                last = v.tensor_scalar(SN[:, a, :], bank[a][:, 0:D + 1], S1[:, a, 1:2], None, ALU.mult)
            last.then_inc(att("sn_ready")[0], 1)
            dve.wait_ge(*att("sc"))
            kk = [HD, HEADS, G]
            chain(v.tensor_reduce(mh[0:HD, 0, :], heads(bank[0][0:HD, :]), AX, ALU.max))
            v.tensor_tensor(heads(AT), heads(bank[0][0:HD, :]), mh[0:HD, 0, :, None].to_broadcast(kk), ALU.subtract).then_inc(att("sc_sub")[0], 1)
            dve.wait_ge(*att("sc_exp"))
            chain(v.tensor_reduce(sh[0:HD, 0, :], heads(AT), AX, ALU.add))
            chain(v.reciprocal(sh[0:HD, 0, :], sh[0:HD, 0, :]))
            v.tensor_tensor(heads(AT), heads(AT), sh[0:HD, 0, :, None].to_broadcast(kk), ALU.mult).then_inc(att("at_sb")[0], 1)
            dve.wait_ge(sem("bout_added"), 1)
            dve.sem_inc(sem("out_free"), 1)
            with dve.Fori(0, CH) as c:
                dve.wait_ge(sem("o_done"), c + 1)
                for b in range(3):
                    w = 2 if b < 2 else 1
                    part = X[:, ds(c * CT + 2 * b, w), :]
                    last = v.tensor_tensor(part, part, bank[b][:, 0:w * D].rearrange("p (j d) -> p j d", j=w), ALU.add)
                last.then_inc(sem("out_free"), 1)


def kernel(**inputs):
    import numpy as _np
    import concourse.bacc as _bacc
    from concourse import mybir as _mybir
    from concourse.bass_utils import run_bass_kernel_spmd as _run

    nc = _bacc.Bacc("TRN2", target_bir_lowering=False, num_devices=1)
    arrays, aps = {}, {}
    for name, value in inputs.items():
        a = _np.ascontiguousarray(value)
        arrays[f"in_{name}_dram"] = a
        aps[name] = nc.dram_tensor(f"in_{name}_dram", a.shape, _mybir.dt.from_np(a.dtype), kind="ExternalInput").ap()
    out = nc.dram_tensor("out_dram", (N, D), _mybir.dt.float32, kind="ExternalOutput").ap()
    gnn_ffn_kernel(nc, aps, out)
    r = _run(nc, [arrays], core_ids=[0])
    return r.results[0]["out_dram"]
```
